# Optimizing a Trainium2 kernel written in Bass

```python
import numpy as np
import jax
import jax.numpy as jnp

def _softmax(x, axis=-1):
    return jax.nn.softmax(x, axis=axis)
def _gelu(x):
    return jax.nn.gelu(x, approximate=True)
def _silu(x):
    return jax.nn.silu(x)
def _sigmoid(x):
    return jax.nn.sigmoid(x)
def _layernorm(x, axis=-1, eps=1e-5):
    m = jnp.mean(x, axis=axis, keepdims=True)
    v = jnp.var(x, axis=axis, keepdims=True)
    return (x - m) / jnp.sqrt(v + eps)
def _scatter_add(tgt, idx, src, axis=0):
    return tgt.at[idx].add(src)
def _segment_sum(src, seg, n):
    return jax.ops.segment_sum(src, seg, n)

kernel_name = 'mk_conv_preact_d1_conv_nchw32_f22e5e'

def setup_inputs(seed: int = 0):
    np.random.seed(seed)
    _w = jnp.asarray
    def _rec_inputs():
        import jax
        import jax.numpy as jnp
        _gk = jax.random.key(seed)
        x = -9.26e-05 + 0.9999 * jax.random.normal(jax.random.fold_in(_gk, 1), (8, 32, 384, 384), jnp.float32)
        return x
    x = _rec_inputs()
    def _L0_conv_setup():
        import jax, jax.numpy as jnp
        import numpy as np
        from jax import lax

        def ste_sign(t):
            return t + lax.stop_gradient(jnp.sign(t) - t)
        key = jax.random.key(seed)
        kx, kw = jax.random.split(key)
        x = jax.random.normal(kx, (8, 32, 384, 384), dtype=jnp.float32)
        W = jax.random.normal(kw, (32, 32, 3, 3), dtype=jnp.float32)
        return {'x': x, 'W': W}
    _L0_conv_all = _L0_conv_setup()
    _L0_conv_in = {k: v for k, v in _L0_conv_all.items() if k in ('W', )}
    del _L0_conv_all

    return {
        "x": x,
        "L0_conv_W": _L0_conv_in["W"],
    }

def reference(x, L0_conv_W):
    import jax
    import jax.numpy as jnp
    def _L0_conv_ref(x, W):
        import jax, jax.numpy as jnp
        import numpy as np
        from jax import lax

        def ste_sign(t):
            return t + lax.stop_gradient(jnp.sign(t) - t)
        xb = ste_sign(x)
        wb = ste_sign(W)
        out = lax.conv_general_dilated(xb, wb, window_strides=(1, 1), padding=[(1, 1), (1, 1)], dimension_numbers=('NCHW', 'OIHW', 'NCHW'))
        return out

    def _gn(v, G=16, eps=1e-5):
        B_, C_, H_, W_ = v.shape
        g = v.reshape(B_, G, C_ // G, H_, W_)
        m = jnp.mean(g, axis=(2, 3, 4), keepdims=True)
        s = jnp.var(g, axis=(2, 3, 4), keepdims=True)
        return ((g - m) / jnp.sqrt(s + eps)).reshape(v.shape)

    def _ln_c(v, eps=1e-6):
        m = jnp.mean(v, axis=1, keepdims=True)
        s = jnp.var(v, axis=1, keepdims=True)
        return (v - m) / jnp.sqrt(s + eps)

    def _ln_t(v, eps=1e-5):
        m = jnp.mean(v, axis=-1, keepdims=True)
        s = jnp.var(v, axis=-1, keepdims=True)
        return (v - m) / jnp.sqrt(s + eps)

    def _to_tokens(v):
        B_, C_, H_, W_ = v.shape
        return v.reshape(B_, C_, H_ * W_).transpose(0, 2, 1)
    def _from_tokens(t, like):
        B_, C_, H_, W_ = like.shape
        return t.transpose(0, 2, 1).reshape(B_, C_, H_, W_)

    x = x + _L0_conv_ref(_gn(x), L0_conv_W)
    return x


_drawn_inputs = setup_inputs


def setup_inputs(seed=0):
    import zlib

    import numpy as np

    out = dict(_drawn_inputs(seed))
    spreads = {}
    factors = {}
    for name, (base, spread) in spreads.items():
        noise = np.random.default_rng([zlib.crc32(name.encode()), seed]).standard_normal(out[name].shape)
        drawn = base * np.exp(spread * noise) if base else spread * noise
        out[name] = jnp.asarray(drawn.astype(out[name].dtype))
    for name, factor in factors.items():
        out[name] = (out[name] * factor).astype(out[name].dtype)
    return out
```

```python
from contextlib import ExitStack

import numpy as np

import concourse.bass as bass
from concourse import mybir

BATCH, CH, H, W = 8, 32, 384, 384
GROUP_CH = 2
TAPS = 3

ROWS = 128 // CH
BLOCKS = 4
CHUNKS = H // (ROWS * BLOCKS)
FREE = BLOCKS * W
TOTAL = BATCH * CHUNKS

UNROLL = 4
GROUPS = CHUNKS // UNROLL
RING = 32
RING_GROUPS = RING // UNROLL
LOAD_LAG = 2
WINDOWS = UNROLL
LEAD = 3
SETS = 2
BANK = 512
PITCH = W + 4
TILE = 64
MEAN_AT = 2

WINDOW_ROWS = ((0, 1, 2, -1), (4, 1, 2, 3))
OUT_ROWS = ((0, 1), (2, 3))


def build(nc, x, weights, same_group, out):
    F32, BF16 = mybir.dt.float32, mybir.dt.bfloat16
    ACT, ALU, AX = mybir.ActivationFunctionType, mybir.AluOpType, mybir.AxisListType
    with ExitStack() as stack:
        sbuf = lambda name, shape, dt: stack.enter_context(nc.sbuf_tensor(name, shape, dt))
        sem = lambda name: stack.enter_context(nc.semaphore(name))

        ring = sbuf("ring", [128, RING, FREE], F32)
        win_a = sbuf("win_a", [128, WINDOWS * BLOCKS, PITCH], BF16)
        win_b = sbuf("win_b", [128, WINDOWS * BLOCKS, PITCH], BF16)
        raw_weights = sbuf("raw_weights", [128, 2 * TAPS * TILE], F32)
        sign_weights = sbuf("sign_weights", [128, 2 * TAPS * TILE], BF16)
        group_matrix = sbuf("group_matrix", [128, 128], F32)
        chunk_sums = sbuf("chunk_sums", [128, CHUNKS], F32)
        image_sum = sbuf("image_sum", [128, 1], F32)
        minus_mean = sbuf("minus_mean", [128, 1], F32)
        psum = [stack.enter_context(nc.psum_tensor(f"psum_{s}", [128, BLOCKS, BANK], F32)) for s in range(SETS)]

        loaded = [sem(f"loaded_{d}") for d in range(UNROLL)]
        stored = [sem(f"stored_{d}") for d in range(UNROLL)]
        constants_in = sem("constants_in")
        windows_zeroed = sem("windows_zeroed")
        summed = sem("summed")
        image_summed = sem("image_summed")
        group_summed = sem("group_summed")
        mean_taken = sem("mean_taken")
        signed = sem("signed")
        rows_copied = sem("rows_copied")
        row_above_ready = sem("row_above_ready")
        row_below_ready = sem("row_below_ready")
        convolved = sem("convolved")
        added = sem("added")

        words_a, words_b = win_a[:].bitcast(F32), win_b[:].bitcast(F32)
        r0, r3, most = slice(0, CH), slice(3 * CH, 4 * CH), slice(0, 3 * CH)
        SLOTS = WINDOWS * BLOCKS

        block = stack.enter_context(nc.Block())

        @block.sync
        def _(sp):
            def load(group, d, slot_group):
                sp.dma_start(ring[:, slot_group * UNROLL + d, :], x[group * UNROLL + d]).then_inc(loaded[d], 16)

            sp.dma_start(raw_weights[:], weights).then_inc(constants_in, 16)
            sp.dma_start(group_matrix[:], same_group).then_inc(constants_in, 16)
            def standing_alone(*waits):
                counts = [(semaphore, sp.to_reg(count)) for semaphore, count in waits]
                sp.wait_ge(constants_in, 32)
                for semaphore, count in counts:
                    sp.wait_ge(semaphore, count)

            def store(group, d):
                sp.dma_start(out[group * UNROLL + d],
                             ring[:, (group % RING_GROUPS) * UNROLL + d, :]).then_inc(stored[d], 16)

            def reload(group, d):
                standing_alone((stored[d], group * 16 + 16), (loaded[d], (group + RING_GROUPS) * 16))
                load(group + RING_GROUPS, d, group % RING_GROUPS)

            for d in range(UNROLL):
                load(0, d, 0)
            with sp.Fori(1, RING_GROUPS) as group:
                for d in range(UNROLL):
                    standing_alone((loaded[d], group * 16))
                    load(group, d, group)

            refills = BATCH * GROUPS - RING_GROUPS
            for d in range(UNROLL):
                sp.wait_ge(added, d + SETS + 1)
                store(0, d)
                if d >= LOAD_LAG:
                    sp.wait_ge(stored[d - LOAD_LAG], 16)
                    sp.wait_ge(loaded[d - LOAD_LAG], RING_GROUPS * 16)
                    load(RING_GROUPS, d - LOAD_LAG, 0)
            with sp.Fori(1, refills) as group:
                for d in range(UNROLL):
                    standing_alone((added, group * UNROLL + (d + SETS + 1)))
                    store(group, d)
                    if d >= LOAD_LAG:
                        reload(group, d - LOAD_LAG)
                    else:
                        reload(group - 1, d - LOAD_LAG + UNROLL)
            for d in range(UNROLL - LOAD_LAG, UNROLL):
                sp.wait_ge(stored[d], refills * 16)
                sp.wait_ge(loaded[d], (BATCH * GROUPS - 1) * 16)
                load(BATCH * GROUPS - 1, d, (refills - 1) % RING_GROUPS)
            with sp.Fori(refills, BATCH * GROUPS) as group:
                for d in range(UNROLL):
                    standing_alone((added, group * UNROLL + (d + SETS + 1)), (stored[d], group * 16))
                    store(group, d)
            for d in range(UNROLL):
                sp.wait_ge(stored[d], BATCH * GROUPS * 16)

        @block.vector
        def _(dve):
            def chunk_sum(group, column_group, d):
                dve.wait_ge(loaded[d], group * 16 + 16)
                nc.vector.tensor_reduce(chunk_sums[:, bass.ds(column_group * UNROLL + d, 1)],
                                        ring[:, (group % RING_GROUPS) * UNROLL + d, :],
                                        AX.X, ALU.add).then_inc(summed, 1)

            def image_total(image):
                dve.wait_ge(summed, (image + 1) * CHUNKS)
                nc.vector.tensor_reduce(image_sum[:], chunk_sums[:], AX.X, ALU.add).then_inc(image_summed, 1)

            def add(group, d):
                n = group * UNROLL + d
                slot = ring[:, (group % RING_GROUPS) * UNROLL + d, :].rearrange("p (k w) -> p k w", k=BLOCKS)
                dve.wait_ge(convolved, n + WINDOWS + 1)
                nc.vector.tensor_tensor(slot, psum[d % SETS][:, :, 0:W], slot, ALU.add).then_inc(added, 1)

            def rows_below(group, d, above=True):
                n = group * UNROLL + d
                k, end = d * BLOCKS, (d + 1) * BLOCKS
                dve.wait_ge(rows_copied, n + 1)
                if d > 0:
                    nc.vector.tensor_copy(win_b[r0, k - 1:end - 1], win_a[r0, k:end]).then_inc(row_below_ready, 1)
                else:
                    if above:
                        nc.vector.tensor_copy(win_b[r0, SLOTS - 1:SLOTS], win_a[r0, 0:1]).then_inc(row_below_ready, 1)
                    nc.vector.tensor_copy(win_b[r0, k:end - 1], win_a[r0, k + 1:end])

            def below_image():
                nc.vector.memset(win_b[r0, SLOTS - 1:SLOTS], 0).then_inc(row_below_ready, 1)

            def image(b, sum_next, sum_after):
                for d in range(LEAD):
                    rows_below(b * GROUPS, d, above=False)
                with dve.Fori(0, GROUPS - 1) as g:
                    for d in range(UNROLL):
                        if d + LEAD < UNROLL:
                            rows_below(b * GROUPS + g, d + LEAD)
                        else:
                            rows_below(b * GROUPS + g + 1, d + LEAD - UNROLL)
                        add(b * GROUPS + g, d)
                        if sum_next:
                            chunk_sum((b + 1) * GROUPS + g + 1, g + 1, d)
                if sum_next:
                    image_total(b + 1)
                    dve.wait_ge(image_summed, b + 2)
                for d in range(UNROLL):
                    if d + LEAD < UNROLL:
                        rows_below(b * GROUPS + (GROUPS - 1), d + LEAD)
                    elif d + LEAD == UNROLL:
                        below_image()
                    add(b * GROUPS + (GROUPS - 1), d)
                    if sum_after:
                        chunk_sum((b + 2) * GROUPS, 0, d)

            dve.sem_inc(added, SETS)
            with dve.Fori(0, GROUPS) as g:
                for d in range(UNROLL):
                    chunk_sum(g, g, d)
            image_total(0)
            dve.wait_ge(image_summed, 1)
            for d in range(UNROLL):
                chunk_sum(GROUPS, 0, d)
            with dve.Fori(0, BATCH - 2) as b:
                image(b, True, True)
            image(BATCH - 2, True, False)
            image(BATCH - 1, False, False)

        @block.scalar
        def _(act):
            act.wait_ge(constants_in, 32)
            nc.scalar.activation(sign_weights[:], raw_weights[:], ACT.Sign).then_inc(signed, 1)
            act.wait_ge(windows_zeroed, 1)

            with act.Fori(0, BATCH) as b:
                act.wait_ge(signed, b * CHUNKS + 1)
                act.wait_ge(group_summed, b + 1)
                nc.scalar.activation(minus_mean[:], psum[0][:, 0, 0:1], ACT.Copy,
                                     scale=-1.0 / (GROUP_CH * H * W)).then_inc(mean_taken, 1)
                act.wait_ge(mean_taken, b + 1)
                with act.Fori(0, GROUPS) as g:
                    for d in range(UNROLL):
                        n = (b * GROUPS + g) * UNROLL + d
                        act.wait_ge(convolved, n + 1)
                        slot = ring[:, ((b * GROUPS + g) % RING_GROUPS) * UNROLL + d, :]
                        nc.scalar.activation(win_b[:, d * BLOCKS:(d + 1) * BLOCKS, 1:1 + W],
                                             slot.rearrange("p (k w) -> p k w", k=BLOCKS),
                                             ACT.Sign, bias=minus_mean[:]).then_inc(signed, 1)
                        act.wait_ge(signed, n + 2)
                        nc.scalar.copy(words_a[most, d * BLOCKS:(d + 1) * BLOCKS],
                                       words_b[most, d * BLOCKS:(d + 1) * BLOCKS]).then_inc(rows_copied, 1)

        @block.gpsimd
        def _(pool):
            nc.gpsimd.memset(words_b, 0)
            nc.gpsimd.memset(words_a, 0).then_inc(windows_zeroed, 1)

            def standing_alone(*waits):
                counts = [(semaphore, pool.to_reg(count)) for semaphore, count in waits]
                pool.wait_ge(windows_zeroed, 1)
                for semaphore, count in counts:
                    pool.wait_ge(semaphore, count)

            def rows_above(group, last):
                for d in range(UNROLL):
                    n = group * UNROLL + d
                    k, end = d * BLOCKS, (d + 1) * BLOCKS
                    standing_alone((signed, n + 2), (convolved, n + WINDOWS - 2))
                    if d < UNROLL - 1:
                        nc.gpsimd.tensor_copy(words_a[r3, k + 1:end + 1], words_b[r3, k:end]).then_inc(row_above_ready, 1)
                    else:
                        if last:
                            nc.gpsimd.memset(words_a[r3, 0:1], 0)
                        else:
                            nc.gpsimd.tensor_copy(words_a[r3, 0:1], words_b[r3, end - 1:end])
                        nc.gpsimd.tensor_copy(words_a[r3, k + 1:end], words_b[r3, k:end - 1]).then_inc(row_above_ready, 1)

            with pool.Fori(0, BATCH) as b:
                with pool.Fori(0, GROUPS - 1) as g:
                    rows_above(b * GROUPS + g, False)
                rows_above(b * GROUPS + (GROUPS - 1), True)

        @block.tensor
        def _(pe):
            def group_sum(image):
                pe.wait_ge(image_summed, image + 1)
                nc.tensor.matmul(psum[0][:, 0, 0:1], group_matrix[:], image_sum[:],
                                 start=True, stop=True).then_inc(group_summed, 1)
                pe.wait_ge(mean_taken, image + 1)

            def convolve(group, d):
                n = group * UNROLL + d
                pe.wait_ge(row_above_ready, n + 1)
                pe.wait_ge(row_below_ready, n + 1)
                for k in range(BLOCKS):
                    for dx in range(TAPS):
                        for tile, window in enumerate((win_a, win_b)):
                            at = (tile * TAPS + dx) * TILE
                            done = nc.tensor.matmul(
                                psum[d % SETS][tile * TILE:(tile + 1) * TILE, k, 0:W],
                                sign_weights[:, at:at + TILE], window[:, d * BLOCKS + k, dx:dx + W],
                                start=(dx == 0), stop=(dx == TAPS - 1))
                done.then_inc(convolved, 1)

            def image(b, mean_next):
                with pe.Fori(0, GROUPS - 1) as g:
                    for d in range(UNROLL):
                        pe.wait_ge(added, (b * GROUPS + g) * UNROLL + d + 1)
                        convolve(b * GROUPS + g, d)
                for d in range(UNROLL):
                    last = b * GROUPS + (GROUPS - 1)
                    pe.wait_ge(added, last * UNROLL + d + 1)
                    if mean_next and d == MEAN_AT:
                        group_sum(b + 1)
                    convolve(last, d)

            pe.sem_inc(convolved, WINDOWS)
            pe.wait_ge(constants_in, 32)
            pe.wait_ge(signed, 1)
            group_sum(0)
            with pe.Fori(0, BATCH - 1) as b:
                image(b, True)
            image(BATCH - 1, False)


def kernel(x, L0_conv_W):
    import concourse.bacc as bacc
    from concourse.bass_utils import run_bass_kernel_spmd

    xs = np.asarray(x).reshape(BATCH, CH, CHUNKS, BLOCKS, ROWS, W).transpose(0, 2, 4, 1, 3, 5)
    xs = np.ascontiguousarray(xs).reshape(TOTAL, 128, FREE)
    w = np.asarray(L0_conv_W)
    ws = np.zeros((ROWS, CH, 2, TAPS, 2, CH), w.dtype)
    for tile in range(2):
        for i, row in enumerate(WINDOW_ROWS[tile]):
            for o, out_row in enumerate(OUT_ROWS[tile]):
                dy = row - out_row + TAPS // 2
                if 0 <= dy < TAPS:
                    ws[i, :, tile, :, o, :] = w[:, :, dy, :].transpose(1, 2, 0)
    ws = ws.reshape(128, 2 * TAPS * TILE)
    group = (np.arange(128) % CH) // GROUP_CH
    same = (group[:, None] == group[None, :]).astype(np.float32)

    nc = bacc.Bacc("TRN2", target_bir_lowering=False, num_devices=1, dynamic_dma_scratch_size=1024)
    F32 = mybir.dt.float32
    x_in = nc.dram_tensor("x_chunks", xs.shape, F32, kind="ExternalInput").ap()
    w_in = nc.dram_tensor("weights", ws.shape, F32, kind="ExternalInput").ap()
    g_in = nc.dram_tensor("same_group", same.shape, F32, kind="ExternalInput").ap()
    o_out = nc.dram_tensor("out_chunks", xs.shape, F32, kind="ExternalOutput").ap()
    build(nc, x_in, w_in, g_in, o_out)
    result = run_bass_kernel_spmd(nc, [{"x_chunks": xs, "weights": ws, "same_group": same}], core_ids=[0])
    o = np.asarray(result.results[0]["out_chunks"]).reshape(BATCH, CHUNKS, ROWS, CH, BLOCKS, W)
    return np.ascontiguousarray(o.transpose(0, 3, 1, 4, 2, 5)).reshape(BATCH, CH, H, W)
```

```python
from contextlib import ExitStack

import numpy as np

import concourse.bass as bass
from concourse import mybir

BATCH, CH, H, W = 8, 32, 384, 384
GROUP_CH = 2
TAPS = 3

ROWS = 128 // CH
BLOCKS = 4
CHUNKS = H // (ROWS * BLOCKS)
FREE = BLOCKS * W
TOTAL = BATCH * CHUNKS

UNROLL = 4
GROUPS = CHUNKS // UNROLL
RING = 32
RING_GROUPS = RING // UNROLL
LOAD_LAG = 1
WINDOWS = UNROLL
LEAD = 3
ACT_D = (1, 3)
ACT_SUMS = GROUPS * len(ACT_D)
SETS = 2
BANK = 512
PITCH = W + 4
TILE = 64
MEAN_AT = 1

WINDOW_ROWS = ((0, 1, 2, -1), (4, 1, 2, 3))
OUT_ROWS = ((0, 1), (2, 3))


def build(nc, x, weights, same_group, out):
    F32, BF16, I32 = mybir.dt.float32, mybir.dt.bfloat16, mybir.dt.int32
    ACT, ALU, AX = mybir.ActivationFunctionType, mybir.AluOpType, mybir.AxisListType
    with ExitStack() as stack:
        sbuf = lambda name, shape, dt: stack.enter_context(nc.sbuf_tensor(name, shape, dt))
        sem = lambda name: stack.enter_context(nc.semaphore(name))

        ring = sbuf("ring", [128, RING, FREE], F32)
        win_a = sbuf("win_a", [128, WINDOWS * BLOCKS, PITCH], BF16)
        win_b = sbuf("win_b", [128, WINDOWS * BLOCKS, PITCH], BF16)
        raw_weights = sbuf("raw_weights", [128, 2 * TAPS * TILE], F32)
        sign_weights = sbuf("sign_weights", [128, 2 * TAPS * TILE], BF16)
        group_matrix = sbuf("group_matrix", [128, 128], F32)
        chunk_sums = sbuf("chunk_sums", [128, CHUNKS], F32)
        not_kept = sbuf("not_kept", [128, FREE], BF16)
        image_sum = sbuf("image_sum", [128, 1], F32)
        minus_mean = sbuf("minus_mean", [128, 1], F32)
        psum = [stack.enter_context(nc.psum_tensor(f"psum_{s}", [128, BLOCKS, BANK], F32)) for s in range(SETS)]

        loaded = [sem(f"loaded_{d}") for d in range(UNROLL)]
        stored = [sem(f"stored_{d}") for d in range(UNROLL)]
        constants_in = sem("constants_in")
        windows_zeroed = sem("windows_zeroed")
        dve_summed = sem("dve_summed")
        act_summed = sem("act_summed")
        image_summed = sem("image_summed")
        group_summed = sem("group_summed")
        mean_taken = sem("mean_taken")
        signed = sem("signed")
        rows_copied = sem("rows_copied")
        windows_ready = sem("windows_ready")
        convolved = sem("convolved")
        added = sem("added")

        words_a, words_b = win_a[:].bitcast(I32), win_b[:].bitcast(I32)
        r0, r3, most = slice(0, CH), slice(3 * CH, 4 * CH), slice(0, 3 * CH)
        SLOTS = WINDOWS * BLOCKS

        block = stack.enter_context(nc.Block())

        @block.sync
        def _(sp):
            def load(group, d, slot_group):
                sp.dma_start(ring[:, slot_group * UNROLL + d, :], x[group * UNROLL + d]).then_inc(loaded[d], 16)

            def standing_alone(*waits):
                counts = [(semaphore, sp.to_reg(count)) for semaphore, count in waits]
                sp.wait_ge(constants_in, 32)
                for semaphore, count in counts:
                    sp.wait_ge(semaphore, count)

            def store(group, d):
                sp.dma_start(out[group * UNROLL + d],
                             ring[:, (group % RING_GROUPS) * UNROLL + d, :]).then_inc(stored[d], 16)

            def reload(group, d):
                standing_alone((stored[d], group * 16 + 16), (loaded[d], (group + RING_GROUPS) * 16))
                load(group + RING_GROUPS, d, group % RING_GROUPS)

            sp.dma_start(raw_weights[:], weights).then_inc(constants_in, 16)
            sp.dma_start(group_matrix[:], same_group).then_inc(constants_in, 16)
            for d in range(UNROLL):
                load(0, d, 0)
            with sp.Fori(1, RING_GROUPS) as group:
                for d in range(UNROLL):
                    standing_alone((loaded[d], group * 16))
                    load(group, d, group)

            refills = BATCH * GROUPS - RING_GROUPS
            for d in range(UNROLL):
                sp.wait_ge(added, d + SETS + 1)
                store(0, d)
                if d >= LOAD_LAG:
                    sp.wait_ge(stored[d - LOAD_LAG], 16)
                    sp.wait_ge(loaded[d - LOAD_LAG], RING_GROUPS * 16)
                    load(RING_GROUPS, d - LOAD_LAG, 0)
            with sp.Fori(1, refills) as group:
                for d in range(UNROLL):
                    standing_alone((added, group * UNROLL + (d + SETS + 1)))
                    store(group, d)
                    if d >= LOAD_LAG:
                        reload(group, d - LOAD_LAG)
                    else:
                        reload(group - 1, d - LOAD_LAG + UNROLL)
            for d in range(UNROLL - LOAD_LAG, UNROLL):
                sp.wait_ge(stored[d], refills * 16)
                sp.wait_ge(loaded[d], (BATCH * GROUPS - 1) * 16)
                load(BATCH * GROUPS - 1, d, (refills - 1) % RING_GROUPS)
            with sp.Fori(refills, BATCH * GROUPS) as group:
                for d in range(UNROLL):
                    standing_alone((added, group * UNROLL + (d + SETS + 1)), (stored[d], group * 16))
                    store(group, d)
            for d in range(UNROLL):
                sp.wait_ge(stored[d], BATCH * GROUPS * 16)

        @block.vector
        def _(dve):
            def chunk_sum(group, column_group, d):
                dve.wait_ge(loaded[d], group * 16 + 16)
                nc.vector.tensor_reduce(chunk_sums[:, bass.ds(column_group * UNROLL + d, 1)],
                                        ring[:, (group % RING_GROUPS) * UNROLL + d, :],
                                        AX.X, ALU.add).then_inc(dve_summed, 1)

            def image_total(image):
                dve.wait_ge(dve_summed, (image + 1) * (CHUNKS - ACT_SUMS))
                dve.wait_ge(act_summed, (image + 1) * ACT_SUMS + 1)
                nc.vector.tensor_reduce(image_sum[:], chunk_sums[:], AX.X, ALU.add).then_inc(image_summed, 1)

            def add(group, d):
                n = group * UNROLL + d
                slot = ring[:, (group % RING_GROUPS) * UNROLL + d, :].rearrange("p (k w) -> p k w", k=BLOCKS)
                dve.wait_ge(convolved, n + WINDOWS + 1)
                nc.vector.tensor_tensor(slot, psum[d % SETS][:, :, 0:W], slot, ALU.add).then_inc(added, 1)

            def copy_rows(group, d, above=True, below=True):
                n = group * UNROLL + d
                k, end = d * BLOCKS, (d + 1) * BLOCKS
                dve.wait_ge(rows_copied, n + 1)
                dve.wait_ge(convolved, n + WINDOWS - 2)
                if d < UNROLL - 1:
                    nc.vector.tensor_copy(win_a[r3, k + 1:end + 1], win_b[r3, k:end])
                else:
                    nc.vector.tensor_copy(win_a[r3, k + 1:end], win_b[r3, k:end - 1])
                    if below:
                        nc.vector.tensor_copy(win_a[r3, 0:1], win_b[r3, end - 1:end])
                    else:
                        nc.vector.memset(win_a[r3, 0:1], 0)
                if d > 0:
                    nc.vector.tensor_copy(win_b[r0, k - 1:end - 1], win_a[r0, k:end]).then_inc(windows_ready, 1)
                else:
                    nc.vector.tensor_copy(win_b[r0, k:end - 1], win_a[r0, k + 1:end])
                    if above:
                        nc.vector.tensor_copy(win_b[r0, SLOTS - 1:SLOTS], win_a[r0, 0:1]).then_inc(windows_ready, 1)
                if not below:
                    nc.vector.memset(win_b[r0, SLOTS - 1:SLOTS], 0).then_inc(windows_ready, 1)

            def image(b, sum_next, sum_after):
                with dve.Fori(0, GROUPS - 1) as g:
                    for d in range(UNROLL):
                        if d + LEAD < UNROLL:
                            copy_rows(b * GROUPS + g, d + LEAD)
                        else:
                            copy_rows(b * GROUPS + g + 1, d + LEAD - UNROLL)
                        add(b * GROUPS + g, d)
                        if sum_next and d not in ACT_D:
                            chunk_sum((b + 1) * GROUPS + g + 1, g + 1, d)
                if sum_next:
                    image_total(b + 1)
                    dve.wait_ge(image_summed, b + 2)
                for d in range(UNROLL):
                    if d + LEAD < UNROLL:
                        copy_rows(b * GROUPS + (GROUPS - 1), d + LEAD, below=(d + LEAD < UNROLL - 1))
                    if sum_next and d + LEAD >= UNROLL:
                        copy_rows((b + 1) * GROUPS, d + LEAD - UNROLL, above=False)
                    add(b * GROUPS + (GROUPS - 1), d)
                    if sum_after and d not in ACT_D:
                        chunk_sum((b + 2) * GROUPS, 0, d)

            dve.sem_inc(added, SETS)
            with dve.Fori(0, GROUPS) as g:
                for d in range(UNROLL):
                    if d not in ACT_D:
                        chunk_sum(g, g, d)
            image_total(0)
            dve.wait_ge(image_summed, 1)
            for d in range(UNROLL):
                if d not in ACT_D:
                    chunk_sum(GROUPS, 0, d)
            for d in range(LEAD):
                copy_rows(0, d, above=False)
            with dve.Fori(0, BATCH - 2) as b:
                image(b, True, True)
            image(BATCH - 2, True, False)
            image(BATCH - 1, False, False)

        @block.scalar
        def _(act):
            act.wait_ge(constants_in, 32)
            nc.scalar.activation(sign_weights[:], raw_weights[:], ACT.Sign).then_inc(signed, 1)
            act.wait_ge(windows_zeroed, 1)

            def chunk_sum(image, g, d):
                group = image * GROUPS + g
                act.wait_ge(loaded[d], group * 16 + 16)
                act.wait_ge(act_summed, group * len(ACT_D) + (ACT_D.index(d) + 1))
                nc.scalar.activation(not_kept[:], ring[:, (group % RING_GROUPS) * UNROLL + d, :], ACT.Identity,
                                     accum_out=chunk_sums[:, bass.ds(g * UNROLL + d, 1)]).then_inc(act_summed, 1)

            def image(b, sum_next):
                act.wait_ge(signed, b * CHUNKS + 1)
                act.wait_ge(group_summed, b + 1)
                nc.scalar.activation(minus_mean[:], psum[MEAN_AT % SETS][:, 0, 0:1], ACT.Copy,
                                     scale=-1.0 / (GROUP_CH * H * W)).then_inc(mean_taken, 1)
                act.wait_ge(mean_taken, b + 1)
                with act.Fori(0, GROUPS) as g:
                    for d in range(UNROLL):
                        n = (b * GROUPS + g) * UNROLL + d
                        act.wait_ge(convolved, n + 1)
                        slot = ring[:, ((b * GROUPS + g) % RING_GROUPS) * UNROLL + d, :]
                        nc.scalar.activation(win_b[:, d * BLOCKS:(d + 1) * BLOCKS, 1:1 + W],
                                             slot.rearrange("p (k w) -> p k w", k=BLOCKS),
                                             ACT.Sign, bias=minus_mean[:]).then_inc(signed, 1)
                        act.wait_ge(signed, n + 2)
                        nc.scalar.copy(words_a[most, d * BLOCKS:(d + 1) * BLOCKS],
                                       words_b[most, d * BLOCKS:(d + 1) * BLOCKS]).then_inc(rows_copied, 1)
                        if sum_next and d in ACT_D:
                            chunk_sum(b + 1, g, d)

            act.sem_inc(act_summed, 1)
            with act.Fori(0, GROUPS) as g:
                for d in ACT_D:
                    chunk_sum(0, g, d)
            with act.Fori(0, BATCH - 1) as b:
                image(b, True)
            image(BATCH - 1, False)

        @block.gpsimd
        def _(pool):
            nc.gpsimd.memset(words_b, 0)
            nc.gpsimd.memset(words_a, 0).then_inc(windows_zeroed, 1)

        @block.tensor
        def _(pe):
            def group_sum(image):
                pe.wait_ge(image_summed, image + 1)
                nc.tensor.matmul(psum[MEAN_AT % SETS][:, 0, 0:1], group_matrix[:], image_sum[:],
                                 start=True, stop=True).then_inc(group_summed, 1)
                pe.wait_ge(mean_taken, image + 1)

            def convolve(group, d):
                n = group * UNROLL + d
                pe.wait_ge(windows_ready, n + 1)
                for k in range(BLOCKS):
                    for dx in range(TAPS):
                        for tile, window in enumerate((win_a, win_b)):
                            at = (tile * TAPS + dx) * TILE
                            done = nc.tensor.matmul(
                                psum[d % SETS][tile * TILE:(tile + 1) * TILE, k, 0:W],
                                sign_weights[:, at:at + TILE], window[:, d * BLOCKS + k, dx:dx + W],
                                start=(dx == 0), stop=(dx == TAPS - 1))
                done.then_inc(convolved, 1)

            def image(b, mean_next):
                with pe.Fori(0, GROUPS - 1) as g:
                    for d in range(UNROLL):
                        pe.wait_ge(added, (b * GROUPS + g) * UNROLL + d + 1)
                        convolve(b * GROUPS + g, d)
                for d in range(UNROLL):
                    last = b * GROUPS + (GROUPS - 1)
                    pe.wait_ge(added, last * UNROLL + d + 1)
                    if mean_next and d == MEAN_AT:
                        group_sum(b + 1)
                    convolve(last, d)

            pe.sem_inc(convolved, WINDOWS)
            pe.wait_ge(constants_in, 32)
            pe.wait_ge(signed, 1)
            group_sum(0)
            with pe.Fori(0, BATCH - 1) as b:
                image(b, True)
            image(BATCH - 1, False)


def kernel(x, L0_conv_W):
    import concourse.bacc as bacc
    from concourse.bass_utils import run_bass_kernel_spmd

    xs = np.asarray(x).reshape(BATCH, CH, CHUNKS, BLOCKS, ROWS, W).transpose(0, 2, 4, 1, 3, 5)
    xs = np.ascontiguousarray(xs).reshape(TOTAL, 128, FREE)
    w = np.asarray(L0_conv_W)
    ws = np.zeros((ROWS, CH, 2, TAPS, 2, CH), w.dtype)
    for tile in range(2):
        for i, row in enumerate(WINDOW_ROWS[tile]):
            for o, out_row in enumerate(OUT_ROWS[tile]):
                dy = row - out_row + TAPS // 2
                if 0 <= dy < TAPS:
                    ws[i, :, tile, :, o, :] = w[:, :, dy, :].transpose(1, 2, 0)
    ws = ws.reshape(128, 2 * TAPS * TILE)
    group = (np.arange(128) % CH) // GROUP_CH
    same = (group[:, None] == group[None, :]).astype(np.float32)

    nc = bacc.Bacc("TRN2", target_bir_lowering=False, num_devices=1, dynamic_dma_scratch_size=1024)
    F32 = mybir.dt.float32
    x_in = nc.dram_tensor("x_chunks", xs.shape, F32, kind="ExternalInput").ap()
    w_in = nc.dram_tensor("weights", ws.shape, F32, kind="ExternalInput").ap()
    g_in = nc.dram_tensor("same_group", same.shape, F32, kind="ExternalInput").ap()
    o_out = nc.dram_tensor("out_chunks", xs.shape, F32, kind="ExternalOutput").ap()
    build(nc, x_in, w_in, g_in, o_out)
    result = run_bass_kernel_spmd(nc, [{"x_chunks": xs, "weights": ws, "same_group": same}], core_ids=[0])
    o = np.asarray(result.results[0]["out_chunks"]).reshape(BATCH, CHUNKS, ROWS, CH, BLOCKS, W)
    return np.ascontiguousarray(o.transpose(0, 3, 1, 4, 2, 5)).reshape(BATCH, CH, H, W)
```
